# Optimizing a Trainium2 kernel written in Bass

```python
import numpy as np
import jax
import jax.numpy as jnp

def _softmax(x, axis=-1):
    return jax.nn.softmax(x, axis=axis)

def _gelu(x):
    return jax.nn.gelu(x, approximate=True)

def _silu(x):
    return jax.nn.silu(x)

def _sigmoid(x):
    return jax.nn.sigmoid(x)

def _layernorm(x, axis=-1, eps=1e-05):
    m = jnp.mean(x, axis=axis, keepdims=True)
    v = jnp.var(x, axis=axis, keepdims=True)
    return (x - m) / jnp.sqrt(v + eps)

def _scatter_add(tgt, idx, src, axis=0):
    return tgt.at[idx].add(src)

def _segment_sum(src, seg, n):
    return jax.ops.segment_sum(src, seg, n)
kernel_name = 'mk_adj_resnorm_d1_adj_r2_32e0d1'

def setup_inputs(seed: int=0):
    np.random.seed(seed)
    _w = jnp.asarray

    def _rec_inputs():
        import jax
        import jax.numpy as jnp
        _gk = jax.random.key(seed)
        x = -8.776e-05 + 1 * jax.random.normal(jax.random.fold_in(_gk, 1), (8192, 128), jnp.float32)
        _a = jax.random.bernoulli(jax.random.fold_in(_gk, 2), 0.000244141, (8192, 8192))
        _a = jnp.logical_or(_a, jnp.eye(8192, dtype=bool))
        _af = _a.astype(jnp.float32)
        _af = _af * jax.random.uniform(jax.random.fold_in(_gk, 3), (8192, 8192), jnp.float32, 0.05, 1)
        adj = _af
        return (x, adj)
    x, adj = _rec_inputs()

    def _L0_gnn_setup():
        import jax, jax.numpy as jnp
        import numpy as np
        N = 10000
        D = 128
        F = 128
        K = F // 8
        key = jax.random.key(seed)
        k1, k2, k3, k4, k5 = jax.random.split(key, 5)
        h = jax.random.normal(k1, (N, D), dtype=jnp.float32)
        adj = jax.random.uniform(k2, (N, N), dtype=jnp.float32)
        W1 = jax.random.normal(k3, (D, K), dtype=jnp.float32) * 0.05
        W2 = jax.random.normal(k4, (K, D, F), dtype=jnp.float32) * 0.05
        b = jax.random.normal(k5, (K, F), dtype=jnp.float32) * 0.05
        return {'h': h, 'adj': adj, 'W1': W1, 'W2': W2, 'b': b}
    _L0_gnn_all = _L0_gnn_setup()
    _L0_gnn_in = {k: v for k, v in _L0_gnn_all.items() if k in ('W1', 'W2', 'b')}
    del _L0_gnn_all
    return {'x': x, 'adj': adj, 'L0_gnn_W1': _L0_gnn_in['W1'], 'L0_gnn_W2': _L0_gnn_in['W2'], 'L0_gnn_b': _L0_gnn_in['b']}

def reference(x, adj, L0_gnn_W1, L0_gnn_W2, L0_gnn_b):
    import jax
    import jax.numpy as jnp

    def _L0_gnn_ref(h, adj, W1, W2, b):
        import jax, jax.numpy as jnp
        import numpy as np
        N = 10000
        D = 128
        F = 128
        K = F // 8
        node = h @ W1
        hw = jnp.einsum('nc,kcf->nkf', h, W2)
        x = jnp.einsum('nk,nkf->nf', node, hw)
        x = adj @ x
        x = x + node @ b
        return jax.nn.relu(x)
    x = _layernorm(x + _L0_gnn_ref(x, adj, L0_gnn_W1, L0_gnn_W2, L0_gnn_b), axis=-1)
    return x

_drawn_inputs = setup_inputs


def setup_inputs(seed=0):
    import zlib

    import numpy as np

    out = dict(_drawn_inputs(seed))
    spreads = {}
    factors = {}
    for name, (base, spread) in spreads.items():
        noise = np.random.default_rng([zlib.crc32(name.encode()), seed]).standard_normal(out[name].shape)
        drawn = base * np.exp(spread * noise) if base else spread * noise
        out[name] = jnp.asarray(drawn.astype(out[name].dtype))
    for name, factor in factors.items():
        out[name] = (out[name] * factor).astype(out[name].dtype)
    return out
```

```python
from contextlib import ExitStack

import concourse.bass as bass
from concourse import mybir

F32 = mybir.dt.float32
ALU = mybir.AluOpType
ACT = mybir.ActivationFunctionType

P = 128
SQ = 32
NG = P // SQ
ROWS = 512
RG = ROWS // SQ
QT = ROWS // P
COLS = 1024
GC = COLS // NG
TC = COLS // P
HT = TC // 2
ARING = 4
TRING = 4
EPS = 1e-05


def graph_norm_kernel(nc, x, adj, W1, W2, b, out):
    N, D = x.shape
    K, _, F = W2.shape
    CH = N // COLS
    NB = N // ROWS
    KB = 512 // F
    KG = K // KB
    CPT = K + 1
    assert D == P and F == P and N % COLS == 0 and NB % 2 == 0

    adj_v = adj.rearrange("(n r i) (c g j) -> n c g i r j", r=RG, i=SQ, c=CH, g=NG)
    x_cols = x.rearrange("(c g t i) d -> c g i t d", g=NG, t=TC, i=SQ)
    x_rows = x.rearrange("(n q p) d -> n p q d", q=QT, p=P)
    out_rows = out.rearrange("(n q p) d -> n p q d", q=QT, p=P)
    node_dram = nc.dram_tensor("node_transposed", [K, N], F32).ap()
    node_store_v = node_dram.rearrange("k (c g h i) -> c h k g i", g=NG, h=2, i=HT * SQ)
    node_load_v = node_dram.rearrange("k (n i) -> n k i", i=ROWS)

    with ExitStack() as ctx:
        def sb(name, shape):
            return ctx.enter_context(nc.sbuf_tensor(name, shape, F32))

        def sem(name):
            return ctx.enter_context(nc.semaphore(name))

        a_ring = sb("a_ring", [P, ARING, RG, GC])
        t_ring = sb("t_ring", [P, TRING, HT, ROWS])
        mix = sb("mix", [P, CH * TC, F])
        w2_sb = sb("w2_sb", [P, K, F])
        w1_sb = sb("w1_sb", [P, K])
        b_sb = sb("b_sb", [K, F])
        ones = sb("ones", [P, P])
        ident = sb("ident", [P, P])
        eps_sb = sb("eps_sb", [P, 1])
        xc = sb("xc", [P, 2, HT, D])
        xT = sb("xT", [P, 2, HT, P])
        node = sb("node", [P, 2, HT, K])
        nodeT = sb("nodeT", [K, 2, NG, HT * SQ])
        part = sb("part", [P, 2, 2, F])
        node_blk = sb("node_blk", [K, 2, ROWS])
        x_blk = sb("x_blk", [P, 2, QT, D])
        relu_sb = sb("relu_sb", [P, ROWS])
        y_sb = sb("y_sb", [P, QT, F])
        o_sb = sb("o_sb", [P, QT, F])
        stats = sb("stats", [P, QT, 6])
        mv = sb("mv", [P, QT, 2])
        std = sb("std", [P, QT])
        rstd = sb("rstd", [P, QT])

        bank = [ctx.enter_context(nc.psum_tensor(f"bank{i}", [P, 512], F32)) for i in range(7)]
        acc = bank[0:2]
        prod = bank[0:4]
        turned_x = bank[4]
        node_ps = bank[5]
        nodeT_ps = bank[6]
        turned_o = bank[6]

        weights_in = sem("weights_in")
        ones_set = sem("ones_set")
        ident_set = sem("ident_set")
        x_in = [sem(f"x_in{h}") for h in range(2)]
        x_turned = sem("x_turned")
        xT_copied = sem("xT_copied")
        node_done = sem("node_done")
        nodeT_copied = sem("nodeT_copied")
        node_copied = sem("node_copied")
        node_stored = [sem(f"node_stored{h}") for h in range(2)]
        prod_done = sem("prod_done")
        combined = sem("combined")
        a_in = [sem(f"a_in{s}") for s in range(ARING)]
        transposed = sem("transposed")
        multiplied = sem("multiplied")
        node_in = [sem(f"node_in{s}") for s in range(2)]
        xb_in = [sem(f"xb_in{s}") for s in range(2)]
        acc_done = sem("acc_done")
        relu_done = sem("relu_done")
        o_turned = sem("o_turned")
        y_done = sem("y_done")
        stats_done = sem("stats_done")
        mv_done = sem("mv_done")
        std_done = sem("std_done")
        rstd_done = sem("rstd_done")
        normed = sem("normed")
        out_stored = sem("out_stored")

        UPC = 2
        UPB = UPC * CH

        def load_adj(eng, blk, c, groups):
            s = c % ARING
            for g in groups:
                eng.dma_start(a_ring[SQ * g:SQ * (g + 1), s], adj_v[blk, c, g]).then_inc(a_in[s], 16)

        def load_x_chunk(eng, c):
            for h in range(2):
                for g in range(NG):
                    eng.dma_start(xc[SQ * g:SQ * (g + 1), h],
                                  x_cols[c, g, :, HT * h:HT * (h + 1), :]).then_inc(x_in[h], 16)

        def next_chunk(blk, c):
            return (blk, c + ARING) if c + ARING < CH else (blk + 1, c + ARING - CH)

        block = ctx.enter_context(nc.Block())

        @block.sync
        def _(sp):
            load_x_chunk(sp, 0)
            sp.dma_start(w1_sb[:], W1).then_inc(weights_in, 16)
            sp.dma_start(w2_sb[:], W2.rearrange("k c f -> c k f")).then_inc(weights_in, 16)
            sp.dma_start(b_sb[:], b).then_inc(weights_in, 16)
            for c in range(ARING):
                load_adj(sp, 0, c, (0, 1))

            def store_node(c, h):
                sp.wait_ge(nodeT_copied, 2 * c + h + 1)
                sp.dma_start(node_store_v[c, h], nodeT[:, h]).then_inc(node_stored[h], 16)

            with sp.Fori(1, CH) as c:
                sp.wait_ge(x_turned, 2 * c)
                load_x_chunk(sp, c)
                for h in range(2):
                    store_node(c - 1, h)
            for h in range(2):
                store_node(CH - 1, h)
            for h in range(2):
                sp.wait_ge(node_stored[h], 16 * CH)

            def step(blk, par, first, last):
                for c in range(CH):
                    if not (last and c + ARING >= CH):
                        sp.wait_ge(transposed, UPB * blk + UPC * (c + 1))
                        load_adj(sp, *next_chunk(blk, c), (0, 1))
                    if c == 0:
                        if not first:
                            sp.wait_ge(acc_done, blk - 1)
                        sp.dma_start(node_blk[:, par], node_load_v[blk]).then_inc(node_in[par], 16)
                    if c == 3:
                        if not first:
                            sp.wait_ge(y_done, blk - 1)
                        sp.dma_start(x_blk[:, par], x_rows[blk]).then_inc(xb_in[par], 16)
                    if c == 7 and not (first and par == 0):
                        store_out(blk - 1)

            def store_out(blk):
                sp.wait_ge(normed, blk + 1)
                sp.dma_start(out_rows[blk], o_sb[:]).then_inc(out_stored, 16)

            for par in range(2):
                step(par, par, True, False)
            with sp.Fori(1, NB // 2 - 1) as pair:
                for par in range(2):
                    step(2 * pair + par, par, False, False)
            for par in range(2):
                step(NB - 2 + par, par, False, par == 1)
            store_out(NB - 1)
            sp.wait_ge(out_stored, 16 * NB)

        @block.gpsimd
        def _(pool):
            nc.gpsimd.memset(eps_sb[:], EPS)
            nc.gpsimd.memset(ones[:], 1.0).then_inc(ones_set, 1)
            pool.wait_ge(ones_set, 1)
            nc.gpsimd.affine_select(out=ident[:], in_=ones[:], compare_op=ALU.is_equal, fill=0.0, base=0,
                                    pattern=[[-1, P]], channel_multiplier=1).then_inc(ident_set, 1)

        @block.scalar
        def _(act):
            for c in range(ARING):
                load_adj(act, 0, c, (2, 3))

            def prepare(c, h, first):
                u = 2 * c + h
                act.wait_ge(x_turned, u + 1)
                if not first:
                    act.wait_ge(prod_done, KG * HT * (u - 1))
                nc.scalar.copy(xT[:, h].rearrange("p t n -> p (t n)"), turned_x[:]).then_inc(xT_copied, 1)
                act.wait_ge(node_done, u + 1)
                if not first:
                    act.wait_ge(node_stored[h], 16 * c)
                nc.scalar.copy(nodeT[:, h].rearrange("k g (t i) -> k t g i", t=HT),
                               nodeT_ps[0:K, :].rearrange("k (t g i) -> k t g i", t=HT, g=NG)
                               ).then_inc(nodeT_copied, 1)
                if not first:
                    act.wait_ge(combined, CPT * HT * (u - 1))
                nc.scalar.copy(node[:, h].rearrange("p t k -> p (t k)"),
                               node_ps[:, 0:HT * K]).then_inc(node_copied, 1)

            for h in range(2):
                prepare(0, h, True)
            with act.Fori(1, CH) as c:
                for h in range(2):
                    prepare(c, h, False)

            def relu(blk, par):
                act.wait_ge(acc_done, blk + 1)
                act.wait_ge(o_turned, blk)
                nc.scalar.activation(relu_sb[:], acc[par][:], ACT.Relu).then_inc(relu_done, 1)

            def deviation(blk):
                act.wait_ge(mv_done, QT * (blk + 1))
                act.wait_ge(rstd_done, blk)
                nc.scalar.activation(std[:], mv[:, :, 1], ACT.Sqrt, bias=eps_sb[:]).then_inc(std_done, 1)

            def step(blk, par, first, last):
                for c in range(CH):
                    if not (last and c + ARING >= CH):
                        act.wait_ge(transposed, UPB * blk + UPC * (c + 1))
                        load_adj(act, *next_chunk(blk, c), (2, 3))
                    if c == 1 and not (first and par == 0):
                        relu(blk - 1, 1 - par)
                    if c == 4 and not (first and par == 0):
                        deviation(blk - 1)

            for par in range(2):
                step(par, par, True, False)
            with act.Fori(1, NB // 2 - 1) as pair:
                for par in range(2):
                    step(2 * pair + par, par, False, False)
            for par in range(2):
                step(NB - 2 + par, par, False, par == 1)
            relu(NB - 1, 1)
            deviation(NB - 1)

        @block.vector
        def _(dve):
            def combine(c, h, t, first):
                u = 2 * c + h
                tile = HT * u + t
                par = t % 2
                for k in range(K):
                    if k % KB == 0:
                        dve.wait_ge(prod_done, KG * tile + k // KB + 1)
                    if not (first and t == 0 and k < 2):
                        dve.wait_ge(combined, CPT * tile + k - 1)
                    src = prod[k // KB][:, F * (k % KB):F * (k % KB + 1)]
                    scale = node[:, h, t, k:k + 1]
                    dst = part[:, par, k % 2]
                    if k < 2:
                        ins = nc.vector.tensor_scalar(dst, src, scale, None, ALU.mult)
                    else:
                        ins = nc.vector.scalar_tensor_tensor(out=dst, in0=src, scalar=scale, in1=dst,
                                                             op0=ALU.mult, op1=ALU.add)
                    ins.then_inc(combined, 1)
                dve.wait_ge(combined, CPT * tile + K)
                nc.vector.tensor_tensor(mix[:, tile, :], part[:, par, 0], part[:, par, 1],
                                        ALU.add).then_inc(combined, 1)

            def combine_chunk(c, first):
                for h in range(2):
                    dve.wait_ge(node_copied, 2 * c + h + 1)
                    for t in range(HT):
                        combine(c, h, t, first and h == 0)

            combine_chunk(0, True)
            with dve.Fori(1, CH) as c:
                combine_chunk(c, False)

            def transpose(blk, c, h, first):
                u = UPB * blk + UPC * c + h
                s = (UPC * c + h) % TRING
                if not (first and UPC * c + h < TRING):
                    dve.wait_ge(multiplied, u - TRING + 1)
                src = a_ring[:, c % ARING].rearrange("p r (t i) -> p t r i", i=SQ)[:, HT * h:HT * (h + 1)]
                nc.vector.transpose(t_ring[:, s].rearrange("p t (r i) -> p t r i", i=SQ), src
                                    ).then_inc(transposed, 1)

            def finish(pair, par, stage):
                blk = 2 * pair + par
                if stage == 0:
                    dve.wait_ge(o_turned, blk + 1)
                    dve.wait_ge(xb_in[par], 16 * (pair + 1))
                    nc.vector.tensor_tensor(y_sb[:].rearrange("p q f -> p (q f)"), turned_o[:],
                                            x_blk[:, par].rearrange("p q f -> p (q f)"), ALU.add
                                            ).then_inc(y_done, 1)
                if stage == 1:
                    dve.wait_ge(y_done, blk + 1)
                    for q in range(QT):
                        nc.vector.bn_stats(stats[:, q], y_sb[:, q]).then_inc(stats_done, 1)
                if stage == 2:
                    for q in range(QT):
                        nc.vector.bn_aggr(mv[:, q], stats[:, q]).then_inc(mv_done, 1)
                if stage == 3:
                    dve.wait_ge(std_done, blk + 1)
                    nc.vector.reciprocal(rstd[:], std[:]).then_inc(rstd_done, 1)
                if stage == 4:
                    dve.wait_ge(rstd_done, blk + 1)
                    dve.wait_ge(out_stored, 16 * blk)
                    for q in range(QT):
                        ins = nc.vector.tensor_scalar(o_sb[:, q], y_sb[:, q], mv[:, q, 0:1],
                                                      rstd[:, q:q + 1], ALU.subtract, ALU.mult)
                    ins.then_inc(normed, 1)

            def before_variances(blk):
                dve.wait_ge(stats_done, QT * (blk + 1))
                dve.wait_ge(std_done, blk)

            STAGE_AT = {8: 0, 9: 1, 10: 2, 12: 3, 14: 4}

            def step(pair, par, first):
                blk = 2 * pair + par
                for c in range(CH):
                    dve.wait_ge(a_in[c % ARING], 16 * NG * (CH // ARING * blk + c // ARING + 1))
                    for h in range(2):
                        stage = STAGE_AT.get(UPC * c + h)
                        if stage == 2 and not first:
                            before_variances(blk - 1)
                        transpose(blk, c, h, first)
                        if stage is not None and not first:
                            finish(pair - 1 + par, 1 - par, stage)

            for par in range(2):
                step(0, par, par == 0)
            with dve.Fori(1, NB // 2) as pair:
                for par in range(2):
                    step(pair, par, False)
            for stage in range(5):
                if stage == 2:
                    before_variances(NB - 1)
                finish(NB // 2 - 1, 1, stage)

        @block.tensor
        def _(pe):
            def turn_x(c, h):
                u = 2 * c + h
                pe.wait_ge(x_in[h], 16 * NG * (c + 1))
                pe.wait_ge(xT_copied, u)
                for t in range(HT):
                    ins = nc.tensor.transpose(turned_x[:, P * t:P * (t + 1)], xc[:, h, t], ident[:])
                ins.then_inc(x_turned, 1)

            def make_node(c, h):
                u = 2 * c + h
                pe.wait_ge(xT_copied, u + 1)
                pe.wait_ge(node_copied, u)
                nc.tensor.matmul(nodeT_ps[0:K, :], w1_sb[:], xT[:, h].rearrange("p t n -> p (t n)"),
                                 start=True, stop=True)
                for t in range(HT):
                    ins = nc.tensor.matmul(node_ps[:, K * t:K * (t + 1)], xT[:, h, t], w1_sb[:],
                                           start=True, stop=True)
                ins.then_inc(node_done, 1)

            def products(c, h, t, first):
                tile = HT * (2 * c + h) + t
                for q in range(KG):
                    if not first:
                        pe.wait_ge(combined, CPT * (tile - 1) + KB * (q + 1))
                    nc.tensor.matmul(prod[q][:], xT[:, h, t],
                                     w2_sb[:, KB * q:KB * (q + 1)].rearrange("p k f -> p (k f)"),
                                     start=True, stop=True).then_inc(prod_done, 1)

            def mix_chunk(c, first, last):
                for h in range(2):
                    for t in range(HT):
                        products(c, h, t, first and h == 0 and t == 0)
                        if not (last and h == 1):
                            if t == 0:
                                turn_x(c + h, 1 - h)
                            if t == 2:
                                make_node(c + h, 1 - h)

            pe.wait_ge(ident_set, 1)
            turn_x(0, 0)
            pe.wait_ge(weights_in, 48)
            make_node(0, 0)
            mix_chunk(0, True, False)
            with pe.Fori(1, CH - 1) as c:
                mix_chunk(c, False, False)
            mix_chunk(CH - 1, False, True)
            pe.wait_ge(combined, CPT * CH * TC)

            def turn_result(blk):
                pe.wait_ge(relu_done, blk + 1)
                pe.wait_ge(y_done, blk)
                for q in range(QT):
                    ins = nc.tensor.transpose(turned_o[:, P * q:P * (q + 1)], relu_sb[:, P * q:P * (q + 1)],
                                              ident[:])
                ins.then_inc(o_turned, 1)

            def step(pair, par, first):
                blk = 2 * pair + par
                if not first:
                    pe.wait_ge(relu_done, blk - 1)
                for c in range(CH):
                    for h in range(2):
                        v = UPC * c + h
                        pe.wait_ge(transposed, UPB * blk + v + 1)
                        for t in range(HT):
                            ins = nc.tensor.matmul(acc[par][:], mix[:, TC * c + HT * h + t],
                                                   t_ring[:, v % TRING, t], start=(v == 0 and t == 0), stop=False)
                        ins.then_inc(multiplied, 1)
                    if c == 1 and not (first and par == 0):
                        turn_result(blk - 1)
                pe.wait_ge(node_in[par], 16 * (pair + 1))
                nc.tensor.matmul(acc[par][:], b_sb[:], node_blk[:, par], start=False, stop=True
                                 ).then_inc(acc_done, 1)

            for par in range(2):
                step(0, par, True)
            with pe.Fori(1, NB // 2) as pair:
                for par in range(2):
                    step(pair, par, False)
            turn_result(NB - 1)


def kernel(x, adj, L0_gnn_W1, L0_gnn_W2, L0_gnn_b):
    import numpy as np
    import concourse.bacc as bacc
    from concourse.bass_utils import run_bass_kernel_spmd

    nc = bacc.Bacc("TRN2", target_bir_lowering=False, num_devices=1)
    arrays = {"x": x, "adj": adj, "W1": L0_gnn_W1, "W2": L0_gnn_W2, "b": L0_gnn_b}
    arrays = {name: np.ascontiguousarray(a) for name, a in arrays.items()}
    ins = [nc.dram_tensor(name, a.shape, mybir.dt.from_np(a.dtype), kind="ExternalInput").ap()
           for name, a in arrays.items()]
    out = nc.dram_tensor("out", x.shape, F32, kind="ExternalOutput").ap()
    graph_norm_kernel(nc, *ins, out)
    return run_bass_kernel_spmd(nc, [arrays], core_ids=[0]).results[0]["out"]
```

```python
from contextlib import ExitStack

import concourse.bass as bass
from concourse import mybir

F32 = mybir.dt.float32
F32R = mybir.dt.float32r
ALU = mybir.AluOpType
ACT = mybir.ActivationFunctionType

P = 128
SQ = 32
NG = P // SQ
ROWS = 512
RG = ROWS // SQ
QT = ROWS // P
COLS = 1024
GC = COLS // NG
TC = COLS // P
HT = TC // 2
SPLIT = 5
LOP = 4
NATIVE = TC - SPLIT
ARING = 4
TRING = 2
SRING = 8
EPS = 1e-05


def graph_norm_kernel(nc, x, adj, W1, W2, b, out):
    N, D = x.shape
    K, _, F = W2.shape
    CH = N // COLS
    NB = N // ROWS
    KB = 512 // F
    KG = K // KB
    ORDER = (0, 2, 1, 3)
    KA = K // 2
    TSTEPS = K - KA + 2
    CSTEPS = TC * TSTEPS + 1
    FOLDS = 3
    assert D == P and F == P and N % COLS == 0 and NB % 2 == 0
    assert KG == len(ORDER) and KA == 8 and LOP == SPLIT - 1
    assert (SPLIT * CH) % SRING == 0 and CH % ARING == 0 and CH % TRING == 0

    adj_v = adj.rearrange("(n r i) (c g j) -> n c g i r j", r=RG, i=SQ, c=CH, g=NG)
    x_cols = x.rearrange("(c g t i) d -> c g i t d", g=NG, t=TC, i=SQ)
    x_rows = x.rearrange("(n q p) d -> n p q d", q=QT, p=P)
    out_rows = out.rearrange("(n q p) d -> n p q d", q=QT, p=P)
    node_dram = nc.dram_tensor("node_transposed", [K, N], F32).ap()
    node_store_v = node_dram.rearrange("k (c g h i) -> c h k g i", g=NG, h=2, i=HT * SQ)
    node_load_v = node_dram.rearrange("k (n i) -> n k i", i=ROWS)

    with ExitStack() as ctx:
        def sem(name):
            return ctx.enter_context(nc.semaphore(name))

        def sb(name, shape, dtype=F32, scope=ctx):
            return scope.enter_context(nc.sbuf_tensor(name, shape, dtype))

        a_ring = sb("a_ring", [P, ARING, RG, GC])
        mix_hi = sb("mix_hi", [P, CH, SPLIT, F], F32R)
        mix_lo = sb("mix_lo", [P, CH, SPLIT, F], F32R)
        mix_f32 = sb("mix_f32", [P, CH, NATIVE, F])
        b_sb = sb("b_sb", [K, F])
        ones = sb("ones", [P, P])
        ident = sb("ident", [P, P])
        eps_sb = sb("eps_sb", [P, 1])
        nodeT = sb("nodeT", [K, 2, NG, HT * SQ])
        node_blk = sb("node_blk", [K, 2, ROWS])
        x_blk = sb("x_blk", [P, 2, QT, D])
        relu_sb = sb("relu_sb", [P, ROWS])
        y_sb = sb("y_sb", [P, QT, F])
        o_sb = sb("o_sb", [P, QT, F])
        stats = sb("stats", [P, QT, 6])
        mv = sb("mv", [P, QT, 2])
        std = sb("std", [P, QT])
        rstd = sb("rstd", [P, QT])

        with ExitStack() as early:
            w2_sb = sb("w2_sb", [P, K, F], scope=early)
            w2_hi = sb("w2_hi", [P, K, F], F32R, early)
            w2_lo = sb("w2_lo", [P, K, F], F32R, early)
            w1_sb = sb("w1_sb", [P, K], scope=early)
            xc = sb("xc", [P, 2, HT, D], scope=early)
            xT = sb("xT", [P, 2, HT, P], scope=early)
            xT_hi = sb("xT_hi", [P, 2, HT, P], F32R, early)
            xT_lo = sb("xT_lo", [P, 2, HT, P], F32R, early)
            node = sb("node", [P, 2, HT, K], scope=early)
            scaled = sb("scaled", [P, 2, KA, F], scope=early)
            folded_sum = sb("folded_sum", [P, 2, F], scope=early)
            part = sb("part", [P, 2, 2, F], scope=early)
            mix_raw = sb("mix_raw", [P, SPLIT, F], scope=early)
        t_ring = sb("t_ring", [P, TRING, TC, ROWS])
        hi_ring = sb("hi_ring", [P, SRING, ROWS], F32R)
        lo_ring = sb("lo_ring", [P, SRING, ROWS], F32R)

        bank = [ctx.enter_context(nc.psum_tensor(f"bank{i}", [P, 512], F32)) for i in range(7)]
        acc = bank[0:2]
        prod = bank[0:4]
        turned_x = bank[4]
        node_ps = bank[5]
        nodeT_ps = bank[6]
        turned_o = bank[6]

        w1_in = sem("w1_in")
        w2_in = sem("w2_in")
        ones_set = sem("ones_set")
        ident_set = sem("ident_set")
        w2_hi_done = sem("w2_hi_done")
        w2_lo_done = sem("w2_lo_done")
        x_in = [sem(f"x_in{h}") for h in range(2)]
        x_turned = sem("x_turned")
        xT_copied = sem("xT_copied")
        xT_hi_done = sem("xT_hi_done")
        xT_lo_done = sem("xT_lo_done")
        node_done = sem("node_done")
        nodeT_copied = sem("nodeT_copied")
        node_copied = sem("node_copied")
        node_stored = [sem(f"node_stored{h}") for h in range(2)]
        prod_done = sem("prod_done")
        scaled_done = sem("scaled_done")
        folded = sem("folded")
        combined = sem("combined")
        mix_hi_done = sem("mix_hi_done")
        a_in = [sem(f"a_in{s}") for s in range(ARING)]
        transposed = sem("transposed")
        hi_done = sem("hi_done")
        lo_pool = sem("lo_pool")
        lo_dve = sem("lo_dve")
        native_used = sem("native_used")
        split_used = sem("split_used")
        node_in = [sem(f"node_in{s}") for s in range(2)]
        xb_in = [sem(f"xb_in{s}") for s in range(2)]
        acc_done = sem("acc_done")
        relu_done = sem("relu_done")
        o_turned = sem("o_turned")
        y_done = sem("y_done")
        stats_done = sem("stats_done")
        mv_done = sem("mv_done")
        std_done = sem("std_done")
        rstd_done = sem("rstd_done")
        normed = sem("normed")
        out_stored = sem("out_stored")

        UPC = 2

        def load_adj(eng, blk, c, groups):
            s = c % ARING
            for g in groups:
                eng.dma_start(a_ring[SQ * g:SQ * (g + 1), s], adj_v[blk, c, g]).then_inc(a_in[s], 16)

        def load_x_chunk(eng, c):
            for h in range(2):
                for g in range(NG):
                    eng.dma_start(xc[SQ * g:SQ * (g + 1), h],
                                  x_cols[c, g, :, HT * h:HT * (h + 1), :]).then_inc(x_in[h], 16)

        def next_chunk(blk, c):
            return (blk, c + ARING) if c + ARING < CH else (blk + 1, c + ARING - CH)

        def combine_steps(c, t):
            return CSTEPS * c + TSTEPS * t

        def before_tile(c, t):
            return (c, t - 1) if t else (c - 1, TC - 1)

        MIX_STEPS = CSTEPS * CH

        block = ctx.enter_context(nc.Block())

        @block.sync
        def _(sp):
            load_x_chunk(sp, 0)
            sp.dma_start(w1_sb[:], W1).then_inc(w1_in, 16)
            sp.dma_start(w2_sb[:], W2.rearrange("k c f -> c k f")).then_inc(w2_in, 16)
            sp.dma_start(b_sb[:], b).then_inc(w2_in, 16)
            for c in range(ARING):
                load_adj(sp, 0, c, (0, 1))

            def store_node(c, h):
                sp.wait_ge(nodeT_copied, 2 * c + h + 1)
                sp.dma_start(node_store_v[c, h], nodeT[:, h]).then_inc(node_stored[h], 16)

            with sp.Fori(1, CH) as c:
                sp.wait_ge(x_turned, 2 * c)
                load_x_chunk(sp, c)
                for h in range(2):
                    store_node(c - 1, h)
            for h in range(2):
                store_node(CH - 1, h)
            for h in range(2):
                sp.wait_ge(node_stored[h], 16 * CH)

            def store_out(blk):
                sp.wait_ge(normed, blk + 1)
                sp.dma_start(out_rows[blk], o_sb[:]).then_inc(out_stored, 16)

            def step(blk, par, first, last):
                for c in range(CH):
                    if not (last and c + ARING >= CH):
                        sp.wait_ge(transposed, UPC * (CH * blk + c + 1))
                        load_adj(sp, *next_chunk(blk, c), (0, 1))
                    if c == 0:
                        if not first:
                            sp.wait_ge(acc_done, blk - 1)
                        sp.dma_start(node_blk[:, par], node_load_v[blk]).then_inc(node_in[par], 16)
                    if c == 3:
                        if not first:
                            sp.wait_ge(y_done, blk - 1)
                        sp.dma_start(x_blk[:, par], x_rows[blk]).then_inc(xb_in[par], 16)
                    if c == CH - 1 and not (first and par == 0):
                        store_out(blk - 1)

            for par in range(2):
                step(par, par, True, False)
            with sp.Fori(1, NB // 2 - 1) as pair:
                for par in range(2):
                    step(2 * pair + par, par, False, False)
            for par in range(2):
                step(NB - 2 + par, par, False, par == 1)
            store_out(NB - 1)
            sp.wait_ge(out_stored, 16 * NB)

        @block.gpsimd
        def _(pool):
            nc.gpsimd.memset(eps_sb[:], EPS)
            nc.gpsimd.memset(ones[:], 1.0).then_inc(ones_set, 1)
            pool.wait_ge(ones_set, 1)
            nc.gpsimd.affine_select(out=ident[:], in_=ones[:], compare_op=ALU.is_equal, fill=0.0, base=0,
                                    pattern=[[-1, P]], channel_multiplier=1).then_inc(ident_set, 1)

            def lo_of_x(c, h, first):
                u = 2 * c + h
                pool.wait_ge(xT_hi_done, u + 1)
                if not first:
                    pool.wait_ge(prod_done, KG * HT * (u - 1))
                nc.gpsimd.tensor_tensor(xT_lo[:, h], xT[:, h], xT_hi[:, h], ALU.subtract).then_inc(xT_lo_done, 1)

            def fold(c, t, first):
                tile = TC * c + t
                par = t % 2
                sc = scaled[:, par]
                pool.wait_ge(scaled_done, KA * (tile + 1))
                nc.gpsimd.tensor_tensor(sc[:, 0:4], sc[:, 0:4], sc[:, 4:8], ALU.add).then_inc(folded, 1)
                pool.wait_ge(folded, FOLDS * tile + 1)
                nc.gpsimd.tensor_tensor(sc[:, 0:2], sc[:, 0:2], sc[:, 2:4], ALU.add).then_inc(folded, 1)
                pool.wait_ge(folded, FOLDS * tile + 2)
                if not (first and t < 2):
                    pool.wait_ge(combined, combine_steps(*before_tile(c, t)))
                nc.gpsimd.tensor_tensor(folded_sum[:, par], sc[:, 0], sc[:, 1], ALU.add).then_inc(folded, 1)

            def fold_chunk(c, first, last):
                for t in range(TC):
                    if t % HT == 1 and not (last and t > HT):
                        h = 1 - t // HT
                        lo_of_x(c + t // HT, h, first and h == 1)
                    fold(c, t, first)

            lo_of_x(0, 0, True)
            fold_chunk(0, True, False)
            with pool.Fori(1, CH - 1) as c:
                fold_chunk(c, False, False)
            fold_chunk(CH - 1, False, True)
            pool.wait_ge(combined, MIX_STEPS)

            def step(blk):
                for c in range(CH):
                    for t in range(LOP):
                        u = CH * blk + c
                        i = SPLIT * u + t
                        s = (SPLIT * c + t) % SRING
                        pool.wait_ge(hi_done, i + 1)
                        if not (isinstance(i, int) and i < SRING):
                            pool.wait_ge(split_used, i - SRING + 1)
                        nc.gpsimd.tensor_tensor(lo_ring[:, s], t_ring[:, c % TRING, t], hi_ring[:, s],
                                                ALU.subtract).then_inc(lo_pool, 1)

            step(0)
            with pool.Fori(1, NB) as blk:
                step(blk)

        @block.scalar
        def _(act):
            for c in range(ARING):
                load_adj(act, 0, c, (2, 3))

            def turned(c, h, first):
                u = 2 * c + h
                act.wait_ge(x_turned, u + 1)
                if not first:
                    act.wait_ge(prod_done, KG * HT * (u - 1))
                    act.wait_ge(xT_lo_done, u - 1)
                nc.scalar.copy(xT[:, h].rearrange("p t n -> p (t n)"), turned_x[:]).then_inc(xT_copied, 1)
                act.wait_ge(xT_copied, u + 1)
                nc.scalar.copy(xT_hi[:, h], xT[:, h]).then_inc(xT_hi_done, 1)

            def nodes(c, h, first):
                u = 2 * c + h
                act.wait_ge(node_done, u + 1)
                if not first:
                    act.wait_ge(scaled_done, KA * HT * (u - 1))
                    act.wait_ge(combined, combine_steps(*((c, 0) if h == 0 else (c, HT)))
                                - TSTEPS * HT - (0 if h else 1))
                nc.scalar.copy(node[:, h].rearrange("p t k -> p (t k)"),
                               node_ps[:, 0:HT * K]).then_inc(node_copied, 1)
                if not first:
                    act.wait_ge(node_stored[h], 16 * c)
                nc.scalar.copy(nodeT[:, h].rearrange("k g (t i) -> k t g i", t=HT),
                               nodeT_ps[0:K, :].rearrange("k (t g i) -> k t g i", t=HT, g=NG)
                               ).then_inc(nodeT_copied, 1)

            def scale(c, t, first):
                tile = TC * c + t
                h, par = t // HT, t % 2
                if t % HT == 0:
                    act.wait_ge(node_copied, 2 * c + h + 1)
                if not (first and t < 2):
                    act.wait_ge(folded, FOLDS * (tile - 1))
                for k in range(KA):
                    if k % KB == 0:
                        act.wait_ge(prod_done, KG * tile + ORDER.index(k // KB) + 1)
                    nc.scalar.activation(scaled[:, par, k], prod[k // KB][:, F * (k % KB):F * (k % KB + 1)],
                                         ACT.Copy, scale=node[:, h, t % HT, k:k + 1]).then_inc(scaled_done, 1)

            def scale_chunk(c, first, last):
                for t in range(TC):
                    scale(c, t, first)
                    if not (last and t >= HT):
                        h = 1 - t // HT
                        if t % HT == 0:
                            turned(c + t // HT, h, first and h == 1)
                        if t % HT == 2:
                            nodes(c + t // HT, h, first and h == 1)
                    if t == SPLIT + 1:
                        act.wait_ge(combined, combine_steps(c, SPLIT))
                        nc.scalar.copy(mix_hi[:, c], mix_raw[:]).then_inc(mix_hi_done, 1)

            turned(0, 0, True)
            act.wait_ge(w2_in, 32)
            for q in ORDER:
                nc.scalar.copy(w2_hi[:, KB * q:KB * (q + 1)], w2_sb[:, KB * q:KB * (q + 1)]).then_inc(w2_hi_done, 1)
            nodes(0, 0, True)
            scale_chunk(0, True, False)
            with act.Fori(1, CH - 1) as c:
                scale_chunk(c, False, False)
            scale_chunk(CH - 1, False, True)
            act.wait_ge(combined, MIX_STEPS)

            def relu(blk, par):
                act.wait_ge(acc_done, blk + 1)
                act.wait_ge(o_turned, blk)
                nc.scalar.activation(relu_sb[:], acc[par][:], ACT.Relu).then_inc(relu_done, 1)

            def deviation(blk):
                act.wait_ge(mv_done, QT * (blk + 1))
                act.wait_ge(rstd_done, blk)
                nc.scalar.activation(std[:], mv[:, :, 1], ACT.Sqrt, bias=eps_sb[:]).then_inc(std_done, 1)

            def step(blk, par, first, last):
                for c in range(CH):
                    u = CH * blk + c
                    act.wait_ge(transposed, UPC * u + 1)
                    for t in range(SPLIT):
                        i = SPLIT * u + t
                        s = (SPLIT * c + t) % SRING
                        if not (isinstance(i, int) and i < SRING):
                            act.wait_ge(split_used, i - SRING + 1)
                        nc.scalar.copy(hi_ring[:, s], t_ring[:, c % TRING, t]).then_inc(hi_done, 1)
                    if not (last and c + ARING >= CH):
                        act.wait_ge(transposed, UPC * (u + 1))
                        load_adj(act, *next_chunk(blk, c), (2, 3))
                    if c == 1 and not (first and par == 0):
                        relu(blk - 1, 1 - par)
                    if c == 4 and not (first and par == 0):
                        deviation(blk - 1)

            for par in range(2):
                step(par, par, True, False)
            with act.Fori(1, NB // 2 - 1) as pair:
                for par in range(2):
                    step(2 * pair + par, par, False, False)
            for par in range(2):
                step(NB - 2 + par, par, False, par == 1)
            relu(NB - 1, 1)
            deviation(NB - 1)

        @block.vector
        def _(dve):
            def combine(c, t, first):
                tile = TC * c + t
                h, par = t // HT, t % 2
                base = combine_steps(c, t)
                for n, k in enumerate(range(KA, K)):
                    if k % KB == 0:
                        dve.wait_ge(prod_done, KG * tile + ORDER.index(k // KB) + 1)
                    if not (first and t == 0 and n < 2):
                        dve.wait_ge(combined, base + n - 1)
                    src = prod[k // KB][:, F * (k % KB):F * (k % KB + 1)]
                    factor = node[:, h, t % HT, k:k + 1]
                    dst = part[:, par, n % 2]
                    if n < 2:
                        ins = nc.vector.tensor_scalar(dst, src, factor, None, ALU.mult)
                    else:
                        ins = nc.vector.scalar_tensor_tensor(out=dst, in0=src, scalar=factor, in1=dst,
                                                             op0=ALU.mult, op1=ALU.add)
                    ins.then_inc(combined, 1)
                dve.wait_ge(combined, base + K - KA)
                nc.vector.tensor_tensor(part[:, par, 0], part[:, par, 0], part[:, par, 1],
                                        ALU.add).then_inc(combined, 1)
                dve.wait_ge(combined, base + K - KA + 1)
                dve.wait_ge(folded, FOLDS * (tile + 1))
                dst = mix_raw[:, t] if t < SPLIT else mix_f32[:, c, t - SPLIT]
                nc.vector.tensor_tensor(dst, part[:, par, 0], folded_sum[:, par], ALU.add).then_inc(combined, 1)

            def combine_chunk(c, first):
                for t in range(TC):
                    if t % HT == 0:
                        dve.wait_ge(node_copied, 2 * c + t // HT + 1)
                    combine(c, t, first)
                dve.wait_ge(mix_hi_done, c + 1)
                nc.vector.tensor_tensor(mix_lo[:, c], mix_raw[:], mix_hi[:, c], ALU.subtract).then_inc(combined, 1)

            for n, q in enumerate(ORDER):
                dve.wait_ge(w2_hi_done, n + 1)
                w = slice(KB * q, KB * (q + 1))
                nc.vector.tensor_tensor(w2_lo[:, w], w2_sb[:, w], w2_hi[:, w], ALU.subtract).then_inc(w2_lo_done, 1)
            combine_chunk(0, True)
            with dve.Fori(1, CH) as c:
                combine_chunk(c, False)
            dve.wait_ge(combined, MIX_STEPS)

            def transpose(u, c, h):
                if not (isinstance(u, int) and u < TRING):
                    if h == 0:
                        dve.wait_ge(hi_done, SPLIT * (u - TRING + 1))
                        dve.wait_ge(lo_pool, LOP * (u - TRING + 1))
                        dve.wait_ge(lo_dve, u - TRING + 1)
                    else:
                        dve.wait_ge(native_used, u - TRING + 1)
                tiles = slice(0, SPLIT) if h == 0 else slice(SPLIT, TC)
                src = a_ring[:, c % ARING].rearrange("p r (t i) -> p t r i", i=SQ)[:, tiles]
                nc.vector.transpose(t_ring[:, c % TRING, tiles].rearrange("p t (r i) -> p t r i", i=SQ), src
                                    ).then_inc(transposed, 1)

            def lo_part(u, c):
                i = SPLIT * u + LOP
                s = (SPLIT * c + LOP) % SRING
                dve.wait_ge(hi_done, i + 1)
                if not (isinstance(i, int) and i < SRING):
                    dve.wait_ge(split_used, i - SRING + 1)
                nc.vector.tensor_tensor(lo_ring[:, s], t_ring[:, c % TRING, LOP], hi_ring[:, s],
                                        ALU.subtract).then_inc(lo_dve, 1)

            def finish(pair, par, stage):
                blk = 2 * pair + par
                if stage == 0:
                    dve.wait_ge(o_turned, blk + 1)
                    dve.wait_ge(xb_in[par], 16 * (pair + 1))
                    nc.vector.tensor_tensor(y_sb[:].rearrange("p q f -> p (q f)"), turned_o[:],
                                            x_blk[:, par].rearrange("p q f -> p (q f)"), ALU.add
                                            ).then_inc(y_done, 1)
                if stage == 1:
                    dve.wait_ge(y_done, blk + 1)
                    for q in range(QT):
                        nc.vector.bn_stats(stats[:, q], y_sb[:, q]).then_inc(stats_done, 1)
                if stage == 2:
                    for q in range(QT):
                        nc.vector.bn_aggr(mv[:, q], stats[:, q]).then_inc(mv_done, 1)
                if stage == 3:
                    dve.wait_ge(std_done, blk + 1)
                    nc.vector.reciprocal(rstd[:], std[:]).then_inc(rstd_done, 1)
                if stage == 4:
                    dve.wait_ge(rstd_done, blk + 1)
                    dve.wait_ge(out_stored, 16 * blk)
                    for q in range(QT):
                        ins = nc.vector.tensor_scalar(o_sb[:, q], y_sb[:, q], mv[:, q, 0:1],
                                                      rstd[:, q:q + 1], ALU.subtract, ALU.mult)
                    ins.then_inc(normed, 1)

            def before_variances(blk):
                dve.wait_ge(stats_done, QT * (blk + 1))
                dve.wait_ge(std_done, blk)

            STAGE_AT = {8: 0, 9: 1, 10: 2, 12: 3, 14: 4}

            def step(pair, par, first):
                blk = 2 * pair + par
                for c in range(CH):
                    u = CH * blk + c
                    dve.wait_ge(a_in[c % ARING], 16 * NG * (CH // ARING * blk + c // ARING + 1))
                    for h in range(2):
                        stage = STAGE_AT.get(UPC * c + h)
                        if stage == 2 and not first:
                            before_variances(blk - 1)
                        transpose(u, c, h)
                        if stage is not None and not first:
                            finish(pair - 1 + par, 1 - par, stage)
                    if not (first and c == 0):
                        lo_part(u - 1, (c - 1) % CH)

            for par in range(2):
                step(0, par, par == 0)
            with dve.Fori(1, NB // 2) as pair:
                for par in range(2):
                    step(pair, par, False)
            lo_part(NB * CH - 1, CH - 1)
            for stage in range(5):
                if stage == 2:
                    before_variances(NB - 1)
                finish(NB // 2 - 1, 1, stage)

        @block.tensor
        def _(pe):
            def turn_x(c, h):
                u = 2 * c + h
                pe.wait_ge(x_in[h], 16 * NG * (c + 1))
                pe.wait_ge(xT_copied, u)
                for t in range(HT):
                    ins = nc.tensor.transpose(turned_x[:, P * t:P * (t + 1)], xc[:, h, t], ident[:])
                ins.then_inc(x_turned, 1)

            def make_node(c, h):
                u = 2 * c + h
                pe.wait_ge(xT_copied, u + 1)
                pe.wait_ge(node_copied, u)
                pe.wait_ge(nodeT_copied, u)
                nc.tensor.matmul(nodeT_ps[0:K, :], w1_sb[:], xT[:, h].rearrange("p t n -> p (t n)"),
                                 start=True, stop=True)
                for t in range(HT):
                    ins = nc.tensor.matmul(node_ps[:, K * t:K * (t + 1)], xT[:, h, t], w1_sb[:],
                                           start=True, stop=True)
                ins.then_inc(node_done, 1)

            def products(c, t, first):
                h = t // HT
                if t % HT == 0:
                    pe.wait_ge(xT_hi_done, 2 * c + h + 1)
                    pe.wait_ge(xT_lo_done, 2 * c + h + 1)
                hi, lo = xT_hi[:, h, t % HT], xT_lo[:, h, t % HT]
                for n, q in enumerate(ORDER):
                    if first and t == 0:
                        pe.wait_ge(w2_lo_done, n + 1)
                    elif q < KG // 2:
                        pe.wait_ge(scaled_done, KA * (TC * c + t - 1) + KB * (q + 1))
                    else:
                        pe.wait_ge(combined, combine_steps(*before_tile(c, t)) + KB * (q - KG // 2 + 1))
                    w = slice(KB * q, KB * (q + 1))
                    w_hi = w2_hi[:, w].rearrange("p k f -> p (k f)")
                    w_lo = w2_lo[:, w].rearrange("p k f -> p (k f)")
                    nc.tensor.matmul(prod[q][:], lo, w_hi, start=True, stop=False)
                    nc.tensor.matmul(prod[q][:], hi, w_lo, start=False, stop=False)
                    nc.tensor.matmul(prod[q][:], hi, w_hi, start=False, stop=True).then_inc(prod_done, 1)

            def mix_chunk(c, first, last):
                for t in range(TC):
                    products(c, t, first)
                    h = 1 - t // HT
                    if not (last and h == 0):
                        if t % HT == 0:
                            turn_x(c + t // HT, h)
                        if t % HT == 1:
                            make_node(c + t // HT, h)

            pe.wait_ge(ident_set, 1)
            turn_x(0, 0)
            pe.wait_ge(w1_in, 16)
            make_node(0, 0)
            mix_chunk(0, True, False)
            with pe.Fori(1, CH - 1) as c:
                mix_chunk(c, False, False)
            mix_chunk(CH - 1, False, True)
            pe.wait_ge(combined, MIX_STEPS)

            def turn_result(blk):
                pe.wait_ge(relu_done, blk + 1)
                pe.wait_ge(y_done, blk)
                for q in range(QT):
                    ins = nc.tensor.transpose(turned_o[:, P * q:P * (q + 1)], relu_sb[:, P * q:P * (q + 1)],
                                              ident[:])
                ins.then_inc(o_turned, 1)

            def step(pair, par, first):
                blk = 2 * pair + par
                if not first:
                    pe.wait_ge(relu_done, blk - 1)
                sums = acc[par][:]
                for c in range(CH):
                    u = CH * blk + c
                    pe.wait_ge(transposed, UPC * (u + 1))
                    for t in range(SPLIT, TC):
                        ins = nc.tensor.matmul(sums, mix_f32[:, c, t - SPLIT], t_ring[:, c % TRING, t],
                                               start=(c == 0 and t == SPLIT), stop=False)
                    ins.then_inc(native_used, 1)
                    for t in range(SPLIT):
                        s = (SPLIT * c + t) % SRING
                        pe.wait_ge(hi_done, SPLIT * u + t + 1)
                        if t < LOP:
                            pe.wait_ge(lo_pool, LOP * u + t + 1)
                        else:
                            pe.wait_ge(lo_dve, u + 1)
                        nc.tensor.matmul(sums, mix_lo[:, c, t], hi_ring[:, s], start=False, stop=False)
                        nc.tensor.matmul(sums, mix_hi[:, c, t], lo_ring[:, s], start=False, stop=False)
                        nc.tensor.matmul(sums, mix_hi[:, c, t], hi_ring[:, s], start=False, stop=False
                                         ).then_inc(split_used, 1)
                    if c == 1 and not (first and par == 0):
                        turn_result(blk - 1)
                pe.wait_ge(node_in[par], 16 * (pair + 1))
                nc.tensor.matmul(sums, b_sb[:], node_blk[:, par], start=False, stop=True
                                 ).then_inc(acc_done, 1)

            for par in range(2):
                step(0, par, True)
            with pe.Fori(1, NB // 2) as pair:
                for par in range(2):
                    step(pair, par, False)
            turn_result(NB - 1)


def kernel(x, adj, L0_gnn_W1, L0_gnn_W2, L0_gnn_b):
    import numpy as np
    import concourse.bacc as bacc
    from concourse.bass_utils import run_bass_kernel_spmd

    nc = bacc.Bacc("TRN2", target_bir_lowering=False, num_devices=1)
    arrays = {"x": x, "adj": adj, "W1": L0_gnn_W1, "W2": L0_gnn_W2, "b": L0_gnn_b}
    arrays = {name: np.ascontiguousarray(a) for name, a in arrays.items()}
    ins = [nc.dram_tensor(name, a.shape, mybir.dt.from_np(a.dtype), kind="ExternalInput").ap()
           for name, a in arrays.items()]
    out = nc.dram_tensor("out", x.shape, F32, kind="ExternalOutput").ap()
    graph_norm_kernel(nc, *ins, out)
    return run_bass_kernel_spmd(nc, [arrays], core_ids=[0]).results[0]["out"]
```

```python
from contextlib import ExitStack

import concourse.bass as bass
from concourse import mybir

F32 = mybir.dt.float32
F32R = mybir.dt.float32r
ALU = mybir.AluOpType
ACT = mybir.ActivationFunctionType

P = 128
SQ = 32
NG = P // SQ
ROWS = 512
RG = ROWS // SQ
QT = ROWS // P
COLS = 1024
GC = COLS // NG
TC = COLS // P
HT = TC // 2
SPLIT = 5
LOP = 4
NATIVE = TC - SPLIT
ARING = 4
TRING = 2
SRING = 8
EPS = 1e-05


def graph_norm_kernel(nc, x, adj, W1, W2, b, out):
    N, D = x.shape
    K, _, F = W2.shape
    CH = N // COLS
    NB = N // ROWS
    KB = 512 // F
    KG = K // KB
    ORDER = (0, 2, 1, 3)
    KA = K // 2
    KV = K - KA
    SUMS = 2
    FOLDS = 2
    assert D == P and F == P and N % COLS == 0 and NB % 2 == 0
    TERMS = 3
    assert TERMS * K <= P and 2 * K == SQ and TC * K == P
    assert KG == len(ORDER) and KA == 8 and LOP == SPLIT - 1
    assert (SPLIT * CH) % SRING == 0 and CH % ARING == 0 and CH % TRING == 0

    adj_v = adj.rearrange("(n r i) (c g j) -> n c g i r j", r=RG, i=SQ, c=CH, g=NG)
    x_cols = x.rearrange("(c g t i) d -> c g i t d", g=NG, t=TC, i=SQ)
    x_rows = x.rearrange("(n q p) d -> n p q d", q=QT, p=P)
    out_rows = out.rearrange("(n q p) d -> n p q d", q=QT, p=P)
    node_dram = nc.dram_tensor("node_transposed", [K, N], F32).ap()
    node_store_v = node_dram.rearrange("k (c g t i) -> c t k g i", g=NG, t=TC, i=SQ)
    node_load_v = node_dram.rearrange("k (n i) -> n k i", i=ROWS)

    with ExitStack() as ctx:
        def sem(name):
            return ctx.enter_context(nc.semaphore(name))

        def sb(name, shape, dtype=F32, scope=ctx):
            return scope.enter_context(nc.sbuf_tensor(name, shape, dtype))

        a_ring = sb("a_ring", [P, ARING, RG, GC])
        mix_hi = sb("mix_hi", [P, CH, SPLIT, F], F32R)
        mix_lo = sb("mix_lo", [P, CH, SPLIT, F], F32R)
        mix_f32 = sb("mix_f32", [P, CH, NATIVE, F])
        mix_raw = sb("mix_raw", [P, SPLIT, F])
        b_sb = sb("b_sb", [TERMS * K, F])
        b_parts = sb("b_parts", [TERMS * K, F], F32R)
        ones = sb("ones", [P, P])
        ident = sb("ident", [P, P])
        eps_sb = sb("eps_sb", [P, 1])
        nodeT = sb("nodeT", [TC * K, P])
        node_blk = sb("node_blk", [TERMS * K, ROWS])
        node_parts = sb("node_parts", [TERMS * K, ROWS], F32R)
        x_blk = sb("x_blk", [P, 2, QT, D])
        relu_sb = sb("relu_sb", [P, ROWS])
        y_sb = sb("y_sb", [P, QT, F])
        o_sb = sb("o_sb", [P, QT, F])
        stats = sb("stats", [P, QT, 6])
        mv = sb("mv", [P, QT, 2])
        std = sb("std", [P, QT])
        rstd = sb("rstd", [P, QT])

        with ExitStack() as early:
            w2_hi = sb("w2_hi", [P, K, F], F32R, early)
            w2_lo = sb("w2_lo", [P, K, F], F32R, early)
            xc = sb("xc", [P, 2, HT, D], scope=early)
            xT = sb("xT", [P, 2, HT, P], scope=early)
            xT_hi = sb("xT_hi", [P, 2, HT, P], F32R, early)
            xT_lo = sb("xT_lo", [P, 2, HT, P], F32R, early)
            w1_sb = sb("w1_sb", [P, K], scope=early)
            node = sb("node", [P, 2, HT, K], scope=early)
            scaled = sb("scaled", [P, 2, KA, F], scope=early)
            w2_sb = scaled[:].rearrange("p s k f -> p (s k) f")
            folded_sum = sb("folded_sum", [P, 2, 2, F], scope=early)
            part = sb("part", [P, 2, 2, F], scope=early)
        hi_ring = sb("hi_ring", [P, SRING, ROWS], F32R)
        lo_ring = sb("lo_ring", [P, SRING, ROWS], F32R)
        t_ring = [sb(f"t_ring{s}", [P, TC, ROWS]) for s in reversed(range(TRING))][::-1]

        bank = [ctx.enter_context(nc.psum_tensor(f"bank{i}", [P, 512], F32)) for i in range(8)]
        acc = bank[0:2]
        prod = [bank[0:4], bank[0:2] + bank[4:6]]
        turned_x = bank[6]
        node_ps = bank[7][:, 0:HT * K]
        nodeT_ps = bank[7][:, P:2 * P]
        turned_o = bank[6]

        w1_in = sem("w1_in")
        w2_in = [sem(f"w2_in{q}") for q in range(KG)]
        b_in = sem("b_in")
        b_hi_done = sem("b_hi_done")
        b_lo_done = sem("b_lo_done")
        ones_set = sem("ones_set")
        ident_set = sem("ident_set")
        w2_hi_done = sem("w2_hi_done")
        w2_lo_done = sem("w2_lo_done")
        x_in = [sem(f"x_in{h}") for h in range(2)]
        x_turned = sem("x_turned")
        xT_copied = sem("xT_copied")
        xT_hi_done = sem("xT_hi_done")
        xT_lo_done = sem("xT_lo_done")
        node_done = sem("node_done")
        node_turned = sem("node_turned")
        nodeT_copied = sem("nodeT_copied")
        node_copied = sem("node_copied")
        node_stored = sem("node_stored")
        prod_done = sem("prod_done")
        scaled_done = sem("scaled_done")
        folded = sem("folded")
        added = sem("added")
        summed = sem("summed")
        mix_lo_done = sem("mix_lo_done")
        mix_hi_done = sem("mix_hi_done")
        a_in = [sem(f"a_in{s}") for s in range(ARING)]
        transposed = sem("transposed")
        hi_done = sem("hi_done")
        lo_pool = sem("lo_pool")
        lo_dve = sem("lo_dve")
        native_used = sem("native_used")
        split_used = sem("split_used")
        node_in = sem("node_in")
        node_hi_done = sem("node_hi_done")
        node_lo_done = sem("node_lo_done")
        xb_in = [sem(f"xb_in{s}") for s in range(2)]
        acc_done = sem("acc_done")
        relu_done = sem("relu_done")
        o_turned = sem("o_turned")
        y_done = sem("y_done")
        stats_done = sem("stats_done")
        mv_done = sem("mv_done")
        std_done = sem("std_done")
        rstd_done = sem("rstd_done")
        normed = sem("normed")
        out_stored = sem("out_stored")

        TURN_AT = 3
        NODE_AT = 3
        UPC = 2

        def load_adj(eng, blk, c, groups):
            s = c % ARING
            for g in groups:
                eng.dma_start(a_ring[SQ * g:SQ * (g + 1), s], adj_v[blk, c, g]).then_inc(a_in[s], 16)

        def load_x_half(eng, c, h):
            for g in range(NG):
                eng.dma_start(xc[SQ * g:SQ * (g + 1), h],
                              x_cols[c, g, :, HT * h:HT * (h + 1), :]).then_inc(x_in[h], 16)

        def next_chunk(blk, c):
            return (blk, c + ARING) if c + ARING < CH else (blk + 1, c + ARING - CH)

        TILES = TC * CH

        block = ctx.enter_context(nc.Block())

        @block.sync
        def _(sp):
            load_x_half(sp, 0, 0)
            sp.dma_start(w1_sb[:], W1).then_inc(w1_in, 16)
            for q in ORDER:
                w = slice(KB * q, KB * (q + 1))
                sp.dma_start(w2_sb[:, w], W2.rearrange("k c f -> c k f")[:, w]).then_inc(w2_in[q], 16)
            load_x_half(sp, 0, 1)
            for term in range(TERMS):
                sp.dma_start(b_sb[K * term:K * (term + 1)], b).then_inc(b_in, 16)
            def store_node(c):
                sp.wait_ge(nodeT_copied, c + 1)
                for t in range(TC):
                    sp.dma_start(node_store_v[c, t], nodeT[K * t:K * (t + 1)].rearrange(
                        "k (g i) -> k g i", g=NG)).then_inc(node_stored, 16)

            def turn_over(c):
                sp.wait_ge(x_turned, 2 * c)
                for h in range(2):
                    load_x_half(sp, c, h)
                store_node(c - 1)

            for c in range(1, 3):
                turn_over(c)
                for a in range(2 * (c - 1), 2 * c):
                    load_adj(sp, 0, a, range(NG))
            with sp.Fori(3, CH) as c:
                turn_over(c)
            sp.wait_ge(transposed, UPC)
            load_adj(sp, 0, ARING, range(NG))
            store_node(CH - 1)
            sp.wait_ge(node_stored, 16 * TC * CH)

            def store_out(blk):
                sp.wait_ge(normed, blk + 1)
                sp.dma_start(out_rows[blk], o_sb[:]).then_inc(out_stored, 16)

            def step(blk, par, first, last):
                for c in range(CH):
                    if not (last and c + ARING >= CH or first and par == 0 and c == 0):
                        sp.wait_ge(transposed, UPC * (CH * blk + c + 1))
                        load_adj(sp, *next_chunk(blk, c), (0, 1))
                    if c == 0:
                        sp.wait_ge(node_lo_done, blk)
                        for term in range(TERMS):
                            sp.dma_start(node_blk[K * term:K * (term + 1)], node_load_v[blk]).then_inc(node_in, 16)
                    if c == 3:
                        if not first:
                            sp.wait_ge(y_done, blk - 1)
                        sp.dma_start(x_blk[:, par], x_rows[blk]).then_inc(xb_in[par], 16)
                    if c == CH - 1 and not (first and par == 0):
                        store_out(blk - 1)

            for par in range(2):
                step(par, par, True, False)
            with sp.Fori(1, NB // 2 - 1) as pair:
                for par in range(2):
                    step(2 * pair + par, par, False, False)
            for par in range(2):
                step(NB - 2 + par, par, False, par == 1)
            store_out(NB - 1)
            sp.wait_ge(out_stored, 16 * NB)

        @block.gpsimd
        def _(pool):
            nc.gpsimd.memset(eps_sb[:], EPS)
            nc.gpsimd.memset(ones[:], 1.0).then_inc(ones_set, 1)
            pool.wait_ge(ones_set, 1)
            nc.gpsimd.affine_select(out=ident[:], in_=ones[:], compare_op=ALU.is_equal, fill=0.0, base=0,
                                    pattern=[[-1, P]], channel_multiplier=1).then_inc(ident_set, 1)

            def lo_of_x(c, h, first):
                u = 2 * c + h
                pool.wait_ge(xT_hi_done, u + 1)
                if not first:
                    pool.wait_ge(prod_done, KG * HT * (u - 1))
                nc.gpsimd.tensor_tensor(xT_lo[:, h], xT[:, h], xT_hi[:, h], ALU.subtract).then_inc(xT_lo_done, 1)

            def fold(c, t, first):
                tile = TC * c + t
                par = t % 2
                sc = scaled[:, par]
                pool.wait_ge(scaled_done, KA * (tile + 1))
                nc.gpsimd.tensor_tensor(sc[:, 0:4], sc[:, 0:4], sc[:, 4:8], ALU.add).then_inc(folded, 1)
                pool.wait_ge(folded, FOLDS * tile + 1)
                if not (first and t < 2):
                    pool.wait_ge(summed, SUMS * (tile - 1))
                nc.gpsimd.tensor_tensor(folded_sum[:, par], sc[:, 0:2], sc[:, 2:4], ALU.add).then_inc(folded, 1)

            def lo_of_mix(c, t0, t1):
                pool.wait_ge(mix_hi_done, c + 1)
                nc.gpsimd.tensor_tensor(mix_lo[:, c, t0:t1], mix_raw[:, t0:t1], mix_hi[:, c, t0:t1],
                                        ALU.subtract).then_inc(mix_lo_done, 1)

            def fold_chunk(c, first, last):
                for t in range(TC):
                    if t % HT == 1 and not (last and t > HT):
                        h = 1 - t // HT
                        lo_of_x(c + t // HT, h, first and h == 1)
                    fold(c, t, first)
                    if t == TC - 2:
                        lo_of_mix(c, 0, 2)
                if not last:
                    lo_of_mix(c, 2, SPLIT)

            lo_of_x(0, 0, True)
            fold_chunk(0, True, False)
            with pool.Fori(1, CH - 1) as c:
                fold_chunk(c, False, False)
            fold_chunk(CH - 1, False, True)
            pool.wait_ge(prod_done, KG * TILES)

            def step(blk, first):
                for c in range(CH):
                    for t in range(LOP):
                        u = CH * blk + c
                        i = SPLIT * u + t
                        s = (SPLIT * c + t) % SRING
                        pool.wait_ge(hi_done, i + 1)
                        if not (isinstance(i, int) and i < SRING):
                            pool.wait_ge(split_used, i - SRING + 1)
                        nc.gpsimd.tensor_tensor(lo_ring[:, s], t_ring[c % TRING][:, t], hi_ring[:, s],
                                                ALU.subtract).then_inc(lo_pool, 1)
                    if first and c == 0:
                        lo_of_mix(CH - 1, 2, SPLIT)
                    if c == NODE_AT:
                        pool.wait_ge(node_hi_done, blk + 1)
                        nc.gpsimd.tensor_tensor(node_parts[0:K], node_blk[0:K], node_parts[0:K],
                                                ALU.subtract).then_inc(node_lo_done, 1)

            step(0, True)
            with pool.Fori(1, NB) as blk:
                step(blk, False)

        @block.scalar
        def _(act):
            def copy_x(c, h, first):
                u = 2 * c + h
                act.wait_ge(x_turned, u + 1)
                if not first:
                    act.wait_ge(prod_done, KG * HT * (u - 1))
                    act.wait_ge(xT_lo_done, u - 1)
                nc.scalar.copy(xT[:, h].rearrange("p t n -> p (t n)"), turned_x[:]).then_inc(xT_copied, 1)

            def hi_of_x(c, h):
                act.wait_ge(xT_copied, 2 * c + h + 1)
                nc.scalar.copy(xT_hi[:, h], xT[:, h]).then_inc(xT_hi_done, 1)

            def copy_node(c, h, first):
                u = 2 * c + h
                act.wait_ge(node_done, u + 1)
                if not first:
                    if h == 0:
                        act.wait_ge(node_turned, c)
                    act.wait_ge(scaled_done, KA * HT * (u - 1))
                    act.wait_ge(added, KV * HT * (u - 1))
                nc.scalar.copy(node[:, h].rearrange("p t k -> p (t k)"),
                               node_ps).then_inc(node_copied, 1)

            def copy_nodeT(c):
                act.wait_ge(node_turned, c + 1)
                act.wait_ge(node_stored, 16 * TC * c)
                nc.scalar.copy(nodeT[:], nodeT_ps).then_inc(nodeT_copied, 1)

            def hi_of_mix(c):
                act.wait_ge(summed, SUMS * (TC * c + SPLIT))
                nc.scalar.copy(mix_hi[:, c], mix_raw[:]).then_inc(mix_hi_done, 1)

            def scale_bank(c, t, q, first):
                tile = TC * c + t
                h, par = t // HT, t % 2
                if t % HT == 0:
                    act.wait_ge(node_copied, 2 * c + h + 1)
                if first and t == 0:
                    act.wait_ge(w2_lo_done, KG)
                if not (first and t < 2):
                    act.wait_ge(folded, FOLDS * (tile - 1))
                act.wait_ge(prod_done, KG * tile + ORDER.index(q) + 1)
                for k in range(KB * q, KB * (q + 1)):
                    nc.scalar.activation(scaled[:, par, k], prod[par][q][:, F * (k % KB):F * (k % KB + 1)],
                                         ACT.Copy, scale=node[:, h, t % HT, k:k + 1]).then_inc(scaled_done, 1)

            def scale_chunk(c, first, last):
                for t in range(TC):
                    scale_bank(c, t, 0, first)
                    h = 1 - t // HT
                    nxt = (c + t // HT, h)
                    more = not (last and h == 0)
                    other = first and h == 1
                    if more and t % HT == 1:
                        hi_of_x(*nxt)
                    if more and t % HT == 2:
                        copy_node(*nxt, other)
                    if t == TURN_AT + 1:
                        copy_nodeT(c)
                    scale_bank(c, t, 1, first)
                    if more and t % HT == 0:
                        copy_x(*nxt, other)
                    if t == SPLIT + 1:
                        hi_of_mix(c)

            copy_x(0, 0, True)
            hi_of_x(0, 0)
            for q in ORDER:
                act.wait_ge(w2_in[q], 16)
                nc.scalar.copy(w2_hi[:, KB * q:KB * (q + 1)], w2_sb[:, KB * q:KB * (q + 1)]).then_inc(w2_hi_done, 1)
            copy_node(0, 0, True)
            act.wait_ge(b_in, 16 * TERMS)
            nc.scalar.copy(b_parts[:], b_sb[:]).then_inc(b_hi_done, 1)
            scale_chunk(0, True, False)
            with act.Fori(1, CH - 1) as c:
                scale_chunk(c, False, False)
            scale_chunk(CH - 1, False, True)
            act.wait_ge(prod_done, KG * TILES)

            def relu(blk, par):
                act.wait_ge(acc_done, blk + 1)
                act.wait_ge(o_turned, blk)
                nc.scalar.activation(relu_sb[:], acc[par][:], ACT.Relu).then_inc(relu_done, 1)

            def deviation(blk):
                act.wait_ge(mv_done, QT * (blk + 1))
                act.wait_ge(rstd_done, blk)
                nc.scalar.activation(std[:], mv[:, :, 1], ACT.Sqrt, bias=eps_sb[:]).then_inc(std_done, 1)

            def step(blk, par, first, last):
                for c in range(CH):
                    u = CH * blk + c
                    act.wait_ge(transposed, UPC * (u + 1))
                    if not (last and c + ARING >= CH or first and par == 0 and c == 0):
                        load_adj(act, *next_chunk(blk, c), (2, 3))
                    for t in range(SPLIT):
                        i = SPLIT * u + t
                        s = (SPLIT * c + t) % SRING
                        if not (isinstance(i, int) and i < SRING):
                            act.wait_ge(split_used, i - SRING + 1)
                        nc.scalar.copy(hi_ring[:, s], t_ring[c % TRING][:, t]).then_inc(hi_done, 1)
                    if c == 1 and not (first and par == 0):
                        relu(blk - 1, 1 - par)
                    if c == NODE_AT:
                        act.wait_ge(node_in, 16 * TERMS * (blk + 1))
                        act.wait_ge(acc_done, blk)
                        nc.scalar.copy(node_parts[:], node_blk[:]).then_inc(node_hi_done, 1)
                    if c == 4 and not (first and par == 0):
                        deviation(blk - 1)

            for par in range(2):
                step(par, par, True, False)
            with act.Fori(1, NB // 2 - 1) as pair:
                for par in range(2):
                    step(2 * pair + par, par, False, False)
            for par in range(2):
                step(NB - 2 + par, par, False, par == 1)
            relu(NB - 1, 1)
            deviation(NB - 1)

        @block.vector
        def _(dve):
            def transpose(u, c, h):
                if not (isinstance(u, int) and u < TRING):
                    if h == 1:
                        dve.wait_ge(hi_done, SPLIT * (u - TRING + 1))
                        dve.wait_ge(lo_pool, LOP * (u - TRING + 1))
                        dve.wait_ge(lo_dve, u - TRING + 1)
                    else:
                        dve.wait_ge(native_used, u - TRING + 1)
                tiles = slice(SPLIT, TC) if h == 0 else slice(0, SPLIT)
                src = a_ring[:, c % ARING].rearrange("p r (t i) -> p t r i", i=SQ)[:, tiles]
                nc.vector.transpose(t_ring[c % TRING][:, tiles].rearrange("p t (r i) -> p t r i", i=SQ), src
                                    ).then_inc(transposed, 1)

            def combine(c, t, first):
                tile = TC * c + t
                h, par = t // HT, t % 2
                if not (first and t < 2):
                    dve.wait_ge(summed, SUMS * (tile - 1))
                for n in range(KV):
                    k = KA + n
                    if k % KB == 0:
                        dve.wait_ge(prod_done, KG * tile + ORDER.index(k // KB) + 1)
                    if not (first and t == 0 and n < 2):
                        dve.wait_ge(added, KV * tile + n - 1)
                    src = prod[par][k // KB][:, F * (k % KB):F * (k % KB + 1)]
                    factor = node[:, h, t % HT, k:k + 1]
                    dst = part[:, par, n % 2]
                    if n < 2:
                        ins = nc.vector.tensor_scalar(dst, src, factor, None, ALU.mult)
                    else:
                        ins = nc.vector.scalar_tensor_tensor(out=dst, in0=src, scalar=factor, in1=dst,
                                                             op0=ALU.mult, op1=ALU.add)
                    ins.then_inc(added, 1)
                    if not (first and t == 0):
                        last_c, last_t = (c, t - 1) if t else (c - 1, TC - 1)
                        if n == KB - 1:
                            join(last_c, last_t)
                        if n == KB + 1:
                            complete(last_c, last_t)

            def first_chunk(n):
                t = (SPLIT + n) % TC
                ins = nc.vector.transpose(t_ring[0][:, t].rearrange("p (r i) -> p r i", i=SQ),
                                          a_ring[:, 0, :, SQ * t:SQ * (t + 1)])
                if t in (TC - 1, SPLIT - 1):
                    ins.then_inc(transposed, 1)

            def join(c, t):
                tile = TC * c + t
                dve.wait_ge(added, KV * (tile + 1))
                dve.wait_ge(folded, FOLDS * (tile + 1))
                nc.vector.tensor_tensor(part[:, t % 2], part[:, t % 2], folded_sum[:, t % 2],
                                        ALU.add).then_inc(summed, 1)

            def complete(c, t):
                dve.wait_ge(summed, SUMS * (TC * c + t) + 1)
                dst = mix_raw[:, t] if t < SPLIT else mix_f32[:, c, t - SPLIT]
                nc.vector.tensor_tensor(dst, part[:, t % 2, 0], part[:, t % 2, 1], ALU.add).then_inc(summed, 1)

            def combine_chunk(c, first, turns_adj):
                for t in range(TC):
                    if t % HT == 0:
                        dve.wait_ge(node_copied, 2 * c + t // HT + 1)
                    if t == 1 and not first:
                        dve.wait_ge(mix_lo_done, 2 * c)
                    combine(c, t, first)
                    if turns_adj:
                        if t == 0:
                            dve.wait_ge(a_in[0], 16 * NG)
                        first_chunk(t)

            for n, q in enumerate(ORDER):
                dve.wait_ge(w2_hi_done, n + 1)
                w = slice(KB * q, KB * (q + 1))
                nc.vector.tensor_tensor(w2_lo[:, w], w2_sb[:, w], w2_hi[:, w], ALU.subtract).then_inc(w2_lo_done, 1)
            dve.wait_ge(b_hi_done, 1)
            rest = slice(K * (TERMS - 1), K * TERMS)
            nc.vector.tensor_tensor(b_parts[rest], b_sb[rest], b_parts[rest], ALU.subtract).then_inc(b_lo_done, 1)
            combine_chunk(0, True, False)
            with dve.Fori(1, CH - 2) as c:
                combine_chunk(c, False, False)
            combine_chunk(CH - 2, False, True)
            combine_chunk(CH - 1, False, False)
            join(CH - 1, TC - 1)
            complete(CH - 1, TC - 1)
            dve.wait_ge(summed, SUMS * TILES)

            def lo_part(u, c):
                i = SPLIT * u + LOP
                s = (SPLIT * c + LOP) % SRING
                dve.wait_ge(hi_done, i + 1)
                if not (isinstance(i, int) and i < SRING):
                    dve.wait_ge(split_used, i - SRING + 1)
                nc.vector.tensor_tensor(lo_ring[:, s], t_ring[c % TRING][:, LOP], hi_ring[:, s],
                                        ALU.subtract).then_inc(lo_dve, 1)

            def finish(pair, par, stage):
                blk = 2 * pair + par
                if stage == 0:
                    dve.wait_ge(o_turned, blk + 1)
                    dve.wait_ge(xb_in[par], 16 * (pair + 1))
                    nc.vector.tensor_tensor(y_sb[:].rearrange("p q f -> p (q f)"), turned_o[:],
                                            x_blk[:, par].rearrange("p q f -> p (q f)"), ALU.add
                                            ).then_inc(y_done, 1)
                if stage == 1:
                    dve.wait_ge(y_done, blk + 1)
                    for q in range(QT):
                        nc.vector.bn_stats(stats[:, q], y_sb[:, q]).then_inc(stats_done, 1)
                if stage == 2:
                    for q in range(QT):
                        nc.vector.bn_aggr(mv[:, q], stats[:, q]).then_inc(mv_done, 1)
                if stage == 3:
                    dve.wait_ge(std_done, blk + 1)
                    nc.vector.reciprocal(rstd[:], std[:]).then_inc(rstd_done, 1)
                if stage == 4:
                    dve.wait_ge(rstd_done, blk + 1)
                    dve.wait_ge(out_stored, 16 * blk)
                    for q in range(QT):
                        ins = nc.vector.tensor_scalar(o_sb[:, q], y_sb[:, q], mv[:, q, 0:1],
                                                      rstd[:, q:q + 1], ALU.subtract, ALU.mult)
                    ins.then_inc(normed, 1)

            def before_variances(blk):
                dve.wait_ge(stats_done, QT * (blk + 1))
                dve.wait_ge(std_done, blk)

            STAGE_AT = {8: 0, 9: 1, 10: 2, 12: 3, 14: 4}

            def step(pair, par, first):
                blk = 2 * pair + par
                for c in range(CH):
                    u = CH * blk + c
                    early = first and c == 0
                    dve.wait_ge(a_in[c % ARING], 16 * NG * (CH // ARING * blk + c // ARING + 1))
                    for h in range(2):
                        stage = STAGE_AT.get(UPC * c + h)
                        if stage == 2 and not first:
                            before_variances(blk - 1)
                        if not early:
                            transpose(u, c, h)
                        if stage is not None and not first:
                            finish(pair - 1 + par, 1 - par, stage)
                    if not (first and c == 0):
                        lo_part(u - 1, (c - 1) % CH)

            for par in range(2):
                step(0, par, par == 0)
            with dve.Fori(1, NB // 2) as pair:
                for par in range(2):
                    step(pair, par, False)
            lo_part(NB * CH - 1, CH - 1)
            for stage in range(5):
                if stage == 2:
                    before_variances(NB - 1)
                finish(NB // 2 - 1, 1, stage)

        @block.tensor
        def _(pe):
            def turn_x(c, h):
                u = 2 * c + h
                pe.wait_ge(x_in[h], 16 * NG * (c + 1))
                pe.wait_ge(xT_copied, u)
                for t in range(HT):
                    ins = nc.tensor.transpose(turned_x[:, P * t:P * (t + 1)], xc[:, h, t], ident[:])
                ins.then_inc(x_turned, 1)

            def make_node(c, h):
                u = 2 * c + h
                pe.wait_ge(xT_copied, u + 1)
                pe.wait_ge(node_copied, u)
                pe.wait_ge(nodeT_copied, c)
                for t in range(HT):
                    ins = nc.tensor.matmul(node_ps[:, K * t:K * (t + 1)], xT[:, h, t], w1_sb[:],
                                           start=True, stop=True)
                ins.then_inc(node_done, 1)

            def turn_node(c):
                pe.wait_ge(node_copied, 2 * c + 2)
                pe.wait_ge(nodeT_copied, c)
                nc.tensor.transpose(nodeT_ps, node[:].rearrange("p h t k -> p (h t k)"), ident[:]
                                    ).then_inc(node_turned, 1)

            def products(c, t, first):
                h = t // HT
                if t % HT == 0:
                    pe.wait_ge(xT_hi_done, 2 * c + h + 1)
                    pe.wait_ge(xT_lo_done, 2 * c + h + 1)
                hi, lo = xT_hi[:, h, t % HT], xT_lo[:, h, t % HT]
                for n, q in enumerate(ORDER):
                    if first and t == 0:
                        pe.wait_ge(w2_lo_done, n + 1)
                    elif q < KG // 2:
                        pe.wait_ge(scaled_done, KA * (TC * c + t - 1) + KB * (q + 1))
                    elif not (first and t < 2):
                        pe.wait_ge(added, KV * (TC * c + t - 2) + KB * (q - KG // 2 + 1))
                    w = slice(KB * q, KB * (q + 1))
                    w_hi = w2_hi[:, w].rearrange("p k f -> p (k f)")
                    w_lo = w2_lo[:, w].rearrange("p k f -> p (k f)")
                    nc.tensor.matmul(prod[t % 2][q][:], lo, w_hi, start=True, stop=False)
                    nc.tensor.matmul(prod[t % 2][q][:], hi, w_lo, start=False, stop=False)
                    nc.tensor.matmul(prod[t % 2][q][:], hi, w_hi, start=False, stop=True).then_inc(prod_done, 1)

            def mix_chunk(c, first, last):
                for t in range(TC):
                    products(c, t, first)
                    h = 1 - t // HT
                    if not (last and h == 0):
                        if t % HT == 0:
                            turn_x(c + t // HT, h)
                        if t % HT == 1:
                            make_node(c + t // HT, h)
                    if t == TURN_AT:
                        turn_node(c)

            pe.wait_ge(ident_set, 1)
            turn_x(0, 0)
            pe.wait_ge(w1_in, 16)
            make_node(0, 0)
            mix_chunk(0, True, False)
            with pe.Fori(1, CH - 1) as c:
                mix_chunk(c, False, False)
            mix_chunk(CH - 1, False, True)
            pe.wait_ge(scaled_done, KA * TILES)
            pe.wait_ge(b_lo_done, 1)
            pe.wait_ge(summed, SUMS * TC)
            pe.wait_ge(mix_lo_done, 2)

            def turn_result(blk):
                pe.wait_ge(relu_done, blk + 1)
                pe.wait_ge(y_done, blk)
                for q in range(QT):
                    ins = nc.tensor.transpose(turned_o[:, P * q:P * (q + 1)], relu_sb[:, P * q:P * (q + 1)],
                                              ident[:])
                ins.then_inc(o_turned, 1)

            def step(pair, par, first):
                blk = 2 * pair + par
                if not first:
                    pe.wait_ge(relu_done, blk - 1)
                sums = acc[par][:]
                for c in range(CH):
                    u = CH * blk + c
                    if first and par == 0 and c == 1:
                        pe.wait_ge(summed, SUMS * TILES)
                        pe.wait_ge(mix_lo_done, 2 * CH)
                    pe.wait_ge(transposed, UPC * u + 1)
                    for t in range(SPLIT, TC):
                        ins = nc.tensor.matmul(sums, mix_f32[:, c, t - SPLIT], t_ring[c % TRING][:, t],
                                               start=(c == 0 and t == SPLIT), stop=False)
                    ins.then_inc(native_used, 1)
                    for t in range(SPLIT):
                        s = (SPLIT * c + t) % SRING
                        pe.wait_ge(hi_done, SPLIT * u + t + 1)
                        if t < LOP:
                            pe.wait_ge(lo_pool, LOP * u + t + 1)
                        else:
                            pe.wait_ge(lo_dve, u + 1)
                        nc.tensor.matmul(sums, mix_lo[:, c, t], hi_ring[:, s], start=False, stop=False)
                        nc.tensor.matmul(sums, mix_hi[:, c, t], lo_ring[:, s], start=False, stop=False)
                        nc.tensor.matmul(sums, mix_hi[:, c, t], hi_ring[:, s], start=False, stop=False
                                         ).then_inc(split_used, 1)
                    if c == 1 and not (first and par == 0):
                        turn_result(blk - 1)
                pe.wait_ge(node_lo_done, blk + 1)
                nc.tensor.matmul(sums, b_parts[:], node_parts[:], start=False, stop=True).then_inc(acc_done, 1)

            for par in range(2):
                step(0, par, True)
            with pe.Fori(1, NB // 2) as pair:
                for par in range(2):
                    step(pair, par, False)
            turn_result(NB - 1)


def kernel(x, adj, L0_gnn_W1, L0_gnn_W2, L0_gnn_b):
    import numpy as np
    import concourse.bacc as bacc
    from concourse.bass_utils import run_bass_kernel_spmd

    nc = bacc.Bacc("TRN2", target_bir_lowering=False, num_devices=1)
    arrays = {"x": x, "adj": adj, "W1": L0_gnn_W1, "W2": L0_gnn_W2, "b": L0_gnn_b}
    arrays = {name: np.ascontiguousarray(a) for name, a in arrays.items()}
    ins = [nc.dram_tensor(name, a.shape, mybir.dt.from_np(a.dtype), kind="ExternalInput").ap()
           for name, a in arrays.items()]
    out = nc.dram_tensor("out", x.shape, F32, kind="ExternalOutput").ap()
    graph_norm_kernel(nc, *ins, out)
    return run_bass_kernel_spmd(nc, [arrays], core_ids=[0]).results[0]["out"]
```
